# Optimizing a Trainium2 kernel written in Bass

```python
import numpy as np
import jax
import jax.numpy as jnp

def _softmax(x, axis=-1):
    return jax.nn.softmax(x, axis=axis)
def _gelu(x):
    return jax.nn.gelu(x, approximate=True)
def _silu(x):
    return jax.nn.silu(x)
def _sigmoid(x):
    return jax.nn.sigmoid(x)
def _layernorm(x, axis=-1, eps=1e-5):
    m = jnp.mean(x, axis=axis, keepdims=True)
    v = jnp.var(x, axis=axis, keepdims=True)
    return (x - m) / jnp.sqrt(v + eps)
def _scatter_add(tgt, idx, src, axis=0):
    return tgt.at[idx].add(src)
def _segment_sum(src, seg, n):
    return jax.ops.segment_sum(src, seg, n)

kernel_name = 'mk_conv_preact_d2_conv_nchw384_e41d68'

def setup_inputs(seed: int = 0):
    np.random.seed(seed)
    _w = jnp.asarray
    def _rec_inputs():
        import jax
        import jax.numpy as jnp
        _gk = jax.random.key(seed)
        x = -0.0001476 + 0.9999 * jax.random.normal(jax.random.fold_in(_gk, 1), (32, 384, 56, 56), jnp.float32)
        return x
    x = _rec_inputs()
    def _L0_conv_setup():
        import jax, jax.numpy as jnp
        import numpy as np
        from jax import lax
        B, C, H, W = (32, 384, 56, 56)
        key = jax.random.key(seed)
        k1, k2, k3, k4 = jax.random.split(key, 4)
        x = jax.random.normal(k1, (B, C, H, W), dtype=jnp.float32)
        pe = 0.02 * jax.random.normal(k2, (1, C, H, 1), dtype=jnp.float32)
        fan_in = H
        bound = 1.0 / np.sqrt(fan_in)
        weight = jax.random.uniform(k3, (C, 1, H, 1), dtype=jnp.float32, minval=-bound, maxval=bound)
        bias = jax.random.uniform(k4, (C,), dtype=jnp.float32, minval=-bound, maxval=bound)
        return {'x': x, 'pe': pe, 'weight': weight, 'bias': bias}
    _L0_conv_all = _L0_conv_setup()
    _L0_conv_in = {k: v for k, v in _L0_conv_all.items() if k in ('pe', 'weight', 'bias', )}
    del _L0_conv_all

    def _L1_conv_setup():
        import jax, jax.numpy as jnp
        import numpy as np
        from jax import lax
        C = 384
        key = jax.random.key(seed)
        k1, k2 = jax.random.split(key)
        x = jax.random.normal(k1, (16, C, 128, 128), dtype=jnp.float32)
        k = jax.random.normal(k2, (C, 1, 3, 3), dtype=jnp.float32)
        return {'x': x, 'k': k}
    _L1_conv_all = _L1_conv_setup()
    _L1_conv_in = {k: v for k, v in _L1_conv_all.items() if k in ('k', )}
    del _L1_conv_all

    return {
        "x": x,
        "L0_conv_pe": _L0_conv_in["pe"],
        "L0_conv_weight": _L0_conv_in["weight"],
        "L0_conv_bias": _L0_conv_in["bias"],
        "L1_conv_k": _L1_conv_in["k"],
    }

def reference(x, L0_conv_pe, L0_conv_weight, L0_conv_bias, L1_conv_k):
    import jax
    import jax.numpy as jnp
    def _L0_conv_ref(x, pe, weight, bias):
        import jax, jax.numpy as jnp
        import numpy as np
        from jax import lax
        B, C, H, W = (32, 384, 56, 56)
        xp = x + pe
        x_cat = jnp.concatenate([xp, xp[:, :, :H - 1, :]], axis=2)
        out = lax.conv_general_dilated(x_cat, weight, window_strides=(1, 1), padding='VALID', dimension_numbers=('NCHW', 'OIHW', 'NCHW'), feature_group_count=C)
        return out + bias[None, :, None, None]

    def _L1_conv_ref(x, k):
        import jax, jax.numpy as jnp
        import numpy as np
        from jax import lax
        C = 384
        return lax.conv_general_dilated(x, k, window_strides=(1, 1), padding=((1, 1), (1, 1)), rhs_dilation=(1, 1), dimension_numbers=('NCHW', 'OIHW', 'NCHW'), feature_group_count=C)

    def _gn(v, G=32, eps=1e-5):
        B_, C_, H_, W_ = v.shape
        g = v.reshape(B_, G, C_ // G, H_, W_)
        m = jnp.mean(g, axis=(2, 3, 4), keepdims=True)
        s = jnp.var(g, axis=(2, 3, 4), keepdims=True)
        return ((g - m) / jnp.sqrt(s + eps)).reshape(v.shape)

    def _ln_c(v, eps=1e-6):
        m = jnp.mean(v, axis=1, keepdims=True)
        s = jnp.var(v, axis=1, keepdims=True)
        return (v - m) / jnp.sqrt(s + eps)

    def _ln_t(v, eps=1e-5):
        m = jnp.mean(v, axis=-1, keepdims=True)
        s = jnp.var(v, axis=-1, keepdims=True)
        return (v - m) / jnp.sqrt(s + eps)

    def _to_tokens(v):
        B_, C_, H_, W_ = v.shape
        return v.reshape(B_, C_, H_ * W_).transpose(0, 2, 1)
    def _from_tokens(t, like):
        B_, C_, H_, W_ = like.shape
        return t.transpose(0, 2, 1).reshape(B_, C_, H_, W_)

    x = x + _L0_conv_ref(_gn(x), L0_conv_pe, L0_conv_weight, L0_conv_bias)
    x = x + _L1_conv_ref(_gn(x), L1_conv_k)
    return x


_drawn_inputs = setup_inputs


def setup_inputs(seed=0):
    import zlib

    import numpy as np

    out = dict(_drawn_inputs(seed))
    spreads = {}
    factors = {'L0_conv_pe': 5.497}
    for name, (base, spread) in spreads.items():
        noise = np.random.default_rng([zlib.crc32(name.encode()), seed]).standard_normal(out[name].shape)
        drawn = base * np.exp(spread * noise) if base else spread * noise
        out[name] = jnp.asarray(drawn.astype(out[name].dtype))
    for name, factor in factors.items():
        out[name] = (out[name] * factor).astype(out[name].dtype)
    return out
```

```python
from contextlib import ExitStack

import concourse.bass as bass
from concourse import mybir


P_ODD = 64
ROWS = 56
KP = P_ODD + ROWS
CG = 12
NB = 16
V = 28
N = NB * V
VP = V + 2
NCH = 384
NGROUP = NCH // CG
HALVES = 2
UNITS = NGROUP * HALVES
BANK = 512
EPS = 1e-5
PAIRS = CG // 2
NX = 4
W_DMAS = 5

F32 = mybir.dt.float32
ALU = mybir.AluOpType
ACT = mybir.ActivationFunctionType


def residual_convs(nc, x_h, t0_h, bias_h, t1_h, pe_h, out_h):
    with ExitStack() as ctx:
        def sb(name, shape):
            return ctx.enter_context(nc.sbuf_tensor(name, shape, F32))

        def ps(name, shape):
            return ctx.enter_context(nc.psum_tensor(name, shape, F32))

        def sem(name):
            return ctx.enter_context(nc.semaphore(name))

        X = [sb(f"X{k}", [128, CG, NB, V]) for k in range(NX)]
        XN0 = sb("XN0", [128, CG, N + 1])
        XN1 = [sb(f"XN1_{k}", [128, CG, NB, VP]) for k in range(2)]
        W0 = [sb(f"W0_{k}", [128, CG, KP]) for k in range(2)]
        W1 = [sb(f"W1_{k}", [128, CG, 4, P_ODD]) for k in range(2)]
        PE = sb("PE", [128, NCH])
        ST = [[sb(f"ST{l}_{k}", [128, NB, 6]) for k in range(2)] for l in range(2)]
        SUM = [sb(f"SUM{l}", [128, NB, 6]) for l in range(2)]
        TMP = [sb(f"TMP{l}", [128, NB, 3]) for l in range(2)]
        MSQ = [sb(f"MSQ{l}", [128, NB]) for l in range(2)]
        VAR = [sb(f"VAR{l}", [128, NB]) for l in range(2)]
        SCALE = [sb(f"SCALE{l}", [128, 2, NB]) for l in range(2)]
        SHIFT = [sb(f"SHIFT{l}", [128, 2, NB]) for l in range(2)]
        AVG = sb("AVG", [128, KP])
        POWER = sb("POWER", [128, NB])

        conv0 = [ps(f"conv0_{k}", [128, BANK]) for k in range(2)]
        conv1 = [ps(f"conv1_{k}", [128, 2, BANK]) for k in range(2)]
        sums = [ps(f"sums{l}", [128, BANK]) for l in range(2)]

        x_loaded = [sem(f"x_loaded{k}") for k in range(NX)]
        x_stored = [sem(f"x_stored{k}") for k in range(NX)]
        w_loaded = [sem(f"w_loaded{k}") for k in range(2)]
        pe_loaded = sem("pe_loaded")
        x_cleared = sem("x_cleared")
        w_cleared = sem("w_cleared")
        xn1_cleared = sem("xn1_cleared")
        pe_filled = sem("pe_filled")
        avg_filled = sem("avg_filled")
        power_filled = sem("power_filled")
        stats_done = [sem(f"stats{l}_done") for l in range(2)]
        squares_done = [sem(f"squares{l}_done") for l in range(2)]
        sums_done = [sem(f"sums{l}_done") for l in range(2)]
        sums_copied = [sem(f"sums{l}_copied") for l in range(2)]
        norm_step = [sem(f"norm{l}_step") for l in range(2)]
        pool_passed = sem("pool_passed")
        norm_ready = [sem(f"norm{l}_ready") for l in range(2)]
        xn_ready = [sem(f"xn{l}_ready") for l in range(2)]
        conv0_done = sem("conv0_done")
        x1_done = sem("x1_done")
        conv1_done = sem("conv1_done")
        x2_done = sem("x2_done")

        block = ctx.enter_context(nc.Block())

        def after(u, n):
            return (u[0] + (u[1] + n) // NX, (u[1] + n) % NX)

        def count(u, each=1, more=0):
            return u[0] * (NX * each) + (u[1] * each + more)

        def slots(eng, slot):
            slot((-1, 3))
            slot((0, 0))
            with eng.Fori(0, (UNITS - NX) // NX) as m:
                for r in range(1, NX + 1):
                    slot((m + r // NX, r % NX), body=True)
            for r in range(1, NX):
                slot((UNITS // NX - 1, r))

        def known(u, body):
            return UNITS // 2 if body else NX * u[0] + u[1]

        def exists(u, n, body):
            return 0 <= known(u, body) + n < UNITS

        @block.sync
        def _(sp):
            def load_x(u):
                k = u[1]
                row = x_h[count(u)]
                sp.dma_start(X[k][0:ROWS].rearrange("p c b v -> p (c b v)"), row[0]).then_inc(x_loaded[k], 16)
                sp.dma_start(X[k][P_ODD:KP].rearrange("p c b v -> p (c b v)"), row[1]).then_inc(x_loaded[k], 16)

            def load_w(g, j):
                done = w_loaded[j]
                sp.dma_start(W0[j][0:ROWS, :, 0:ROWS], t0_h[g]).then_inc(done, 16)
                sp.dma_start(W0[j][P_ODD:KP, :, P_ODD:KP], t0_h[g]).then_inc(done, 16)
                sp.dma_start(W0[j][ROWS:ROWS + 1, :, :], bias_h[g]).then_inc(done, 16)
                sp.dma_start(W1[j][0:ROWS, :, 1:4, :].rearrange("p c s i -> p c (s i)"),
                             t1_h[g][:, :, 0:3, :].rearrange("p c s i -> p c (s i)")).then_inc(done, 16)
                sp.dma_start(W1[j][P_ODD:KP, :, 0:3, :].rearrange("p c s i -> p c (s i)"),
                             t1_h[g][:, :, 1:4, :].rearrange("p c s i -> p c (s i)")).then_inc(done, 16)

            def store(u):
                k = u[1]
                sp.wait_ge(x2_done, count(u, PAIRS, PAIRS))
                row = out_h[count(u)]
                sp.dma_start(row[0], X[k][0:ROWS].rearrange("p c b v -> p (c b v)")).then_inc(x_stored[k], 16)
                sp.dma_start(row[1], X[k][P_ODD:KP].rearrange("p c b v -> p (c b v)")).then_inc(x_stored[k], 16)

            def store_and_reload(u):
                store(u)
                if u[1] % 2:
                    load_w(u[0] * 2 + (u[1] // 2 + 2), u[1] // 2)
                sp.wait_ge(x_stored[u[1]], 32 * u[0] + 32)
                load_x(after(u, NX))

            sp.wait_ge(x_cleared, 1)
            load_x((0, 0))
            sp.wait_ge(pe_filled, 1)
            sp.dma_start(PE[0:ROWS, :], pe_h).then_inc(pe_loaded, 16)
            sp.dma_start(PE[P_ODD:KP, :], pe_h).then_inc(pe_loaded, 16)
            sp.wait_ge(w_cleared, 4)
            load_w(0, 0)
            for k in range(1, NX):
                sp.wait_ge(x_cleared, k + 1)
                load_x((0, k))
                if k == 1:
                    load_w(1, 1)
            with sp.Fori(0, UNITS // NX - 1) as m:
                for r in range(NX):
                    store_and_reload((m, r))
            for r in range(NX):
                store((UNITS // NX - 1, r))
            for k in range(NX):
                sp.wait_ge(x_stored[k], 32 * (UNITS // NX))

        @block.vector
        def _(dve):
            nc.vector.memset(X[0][:], 0.0).then_inc(x_cleared, 1)
            for k in range(2):
                nc.vector.memset(W0[k][:], 0.0).then_inc(w_cleared, 1)
                nc.vector.memset(W1[k][:], 0.0).then_inc(w_cleared, 1)
            for k in range(1, NX):
                nc.vector.memset(X[k][:], 0.0).then_inc(x_cleared, 1)

            def statistics(l, u, body, images):
                for b in images:
                    if b == 0:
                        if l == 0:
                            dve.wait_ge(x_loaded[u[1]], 32 * u[0] + 32)
                        else:
                            dve.wait_ge(x1_done, count(u, CG, CG))
                        if known(u, body) >= 2:
                            dve.wait_ge(sums_done[l], count(u, 1, -1))
                    last = nc.vector.bn_stats(ST[l][u[1] % 2][0:KP, b, :], X[u[1]][0:KP, :, b, :])
                    if b == NB - 1:
                        last.then_inc(stats_done[l], 1)

            def add_conv0(u, c):
                bank = conv0[c % 2]
                dve.wait_ge(conv0_done, count(u, CG, c + 1))
                x = X[u[1]][0:KP, c].rearrange("p b v -> p (b v)")
                nc.vector.scalar_tensor_tensor(out=x, in0=bank[0:KP, 0:N], scalar=bank[0:KP, N:N + 1], in1=x,
                                               op0=ALU.add, op1=ALU.add).then_inc(x1_done, 1)

            def add_conv1(u, j):
                dve.wait_ge(conv1_done, count(u, PAIRS, j + 1))
                x = X[u[1]][0:KP, 2 * j:2 * j + 2].rearrange("p c b v -> p c (b v)")
                nc.vector.tensor_tensor(x, conv1[j % 2][0:KP, :, 0:N], x, ALU.add).then_inc(x2_done, 1)

            def slot(u, body=False):
                if exists(u, 1, body):
                    for c in range(CG):
                        add_conv0(after(u, 1), c)
                for j in range(PAIRS):
                    if exists(u, 1, body):
                        if j < 3:
                            statistics(1, after(u, 1), body, range(NB * j // 3, NB * (j + 1) // 3))
                    if exists(u, 0, body):
                        add_conv1(u, j)
                if exists(u, 3, body):
                    statistics(0, after(u, 3), body, range(NB))

            for k in range(2):
                statistics(0, (0, k), False, range(NB))
            slots(dve, slot)

        def sum_statistics(pe, l, u, body):
            pe.wait_ge(squares_done[l], count(u, 1, 1))
            if known(u, body) >= 1:
                pe.wait_ge(sums_copied[l], count(u))
            nc.tensor.matmul(sums[l][0:KP, 0:NB * 6], AVG[0:KP, :],
                             ST[l][u[1] % 2][0:KP].rearrange("p b s -> p (b s)"),
                             start=True, stop=True).then_inc(sums_done[l], 1)

        @block.tensor
        def _(pe):
            def layer0(u, body, c):
                g = (u[1] // 2) % 2
                if c == 0:
                    pe.wait_ge(xn_ready[0], count(u, 1, 1))
                    pe.wait_ge(w_loaded[g], 16 * W_DMAS * u[0] + 16 * W_DMAS)
                if known(u, body) * CG + c >= 2:
                    pe.wait_ge(x1_done, count(u, CG, c - 1))
                nc.tensor.matmul(conv0[c % 2][0:KP, 0:N + 1], W0[g][0:KP, c, :], XN0[0:KP, c, :],
                                 start=True, stop=True).then_inc(conv0_done, 1)

            def layer1(u, body, j):
                g = (u[1] // 2) % 2
                if j == 0:
                    pe.wait_ge(xn_ready[1], count(u, 1, 1))
                if known(u, body) * PAIRS + j >= 2:
                    pe.wait_ge(x2_done, count(u, PAIRS, j - 1))
                for i in range(2):
                    c = 2 * j + i
                    even = conv1[j % 2][0:P_ODD, i, 0:N]
                    odd = conv1[j % 2][P_ODD:KP, i, 0:N]
                    for part in range(2):
                        for out, side in ((even, 0), (odd, 1)):
                            last = nc.tensor.matmul(out, W1[g][0:KP, c, 2 * side + part, 0:out.shape[0]],
                                                    XN1[u[1] % 2][0:KP, c, :, side + part:side + part + V],
                                                    start=part == 0, stop=part == 1)
                last.then_inc(conv1_done, 1)

            def slot(u, body=False):
                if exists(u, 1, body):
                    for c in range(CG):
                        layer0(after(u, 1), body, c)
                        if c == 3 and exists(u, 2, body):
                            sum_statistics(pe, 0, after(u, 2), body)
                for j in range(PAIRS):
                    if exists(u, 0, body):
                        layer1(u, body, j)
                    if j == 3 and exists(u, 1, body):
                        sum_statistics(pe, 1, after(u, 1), body)

            pe.wait_ge(avg_filled, 3)
            sum_statistics(pe, 0, (0, 0), False)
            pe.wait_ge(xn1_cleared, 2)
            pe.wait_ge(pe_loaded, 32)
            slots(pe, slot)

        @block.scalar
        def _(act):
            def squares(l, u):
                st = ST[l][u[1] % 2][0:KP].rearrange("p b (a s) -> p b a s", a=2)
                act.wait_ge(stats_done[l], count(u, 1, 1))
                nc.scalar.activation(st[:, :, :, 0], st[:, :, :, 1], ACT.Square,
                                     scale=float(CG * V / 2) ** 0.5).then_inc(squares_done[l], 1)

            def copy_sums(l, u, body):
                act.wait_ge(sums_done[l], count(u, 1, 1))
                if known(u, body) >= 1:
                    act.wait_ge(norm_ready[l], count(u))
                nc.scalar.activation(SUM[l][0:KP].rearrange("p b s -> p (b s)"), sums[l][0:KP, 0:NB * 6],
                                     ACT.Copy).then_inc(sums_copied[l], 1)

            def normalise(u, body, images):
                for b in images:
                    if b == 0:
                        act.wait_ge(norm_ready[1], count(u, 1, 1))
                        if known(u, body) >= 2:
                            act.wait_ge(conv1_done, count(u, PAIRS, -PAIRS))
                    last = nc.scalar.activation(XN1[u[1] % 2][0:KP, :, b, 1:1 + V], X[u[1]][0:KP, :, b, :],
                                                ACT.Identity, bias=SHIFT[1][0:KP, u[1] % 2, b:b + 1],
                                                scale=SCALE[1][0:KP, u[1] % 2, b:b + 1])
                    if b == NB - 1:
                        last.then_inc(xn_ready[1], 1)

            def slot(u, body=False):
                if exists(u, 1, body):
                    squares(1, after(u, 1))
                    copy_sums(1, after(u, 1), body)
                    normalise(after(u, 1), body, range(8))
                if exists(u, 3, body):
                    squares(0, after(u, 3))
                if exists(u, 1, body):
                    normalise(after(u, 1), body, range(8, 14))
                if exists(u, 3, body):
                    copy_sums(0, after(u, 3), body)
                if exists(u, 1, body):
                    normalise(after(u, 1), body, range(14, NB))

            act.wait_ge(xn1_cleared, 2)
            for k in range(2):
                squares(0, (0, k))
                copy_sums(0, (0, k), False)
            slots(act, slot)

        @block.gpsimd
        def _(pool):
            nc.gpsimd.memset(AVG[:, 0:ROWS], -1.0 / (2 * 2 * ROWS)).then_inc(avg_filled, 1)
            nc.gpsimd.memset(AVG[:, ROWS:P_ODD], 0.0).then_inc(avg_filled, 1)
            nc.gpsimd.memset(AVG[:, P_ODD:KP], -1.0 / (2 * 2 * ROWS)).then_inc(avg_filled, 1)
            nc.gpsimd.memset(PE[:], 1.0).then_inc(pe_filled, 1)
            nc.gpsimd.memset(POWER[:], -0.5).then_inc(power_filled, 1)
            for k in range(2):
                nc.gpsimd.memset(XN1[k][:], 0.0).then_inc(xn1_cleared, 1)
            pool.wait_ge(power_filled, 1)
            pool.wait_ge(pe_loaded, 32)
            STEPS = 7

            def wait_alone(sem, value):
                pool.wait_ge(sem, value)
                pool.sem_inc(pool_passed, 1)

            def scale_and_shift(l, u, body):
                steps = [0]

                def step(instruction):
                    instruction.then_inc(norm_step[l], 1)
                    steps[0] += 1
                    wait_alone(norm_step[l], count(u, STEPS, steps[0]))

                pool.wait_ge(sums_copied[l], count(u, 1, 1))
                if l == 1 and known(u, body) >= 2:
                    pool.wait_ge(xn_ready[1], count(u, 1, -1))
                s, t = SUM[l][0:KP], TMP[l][0:KP]
                msq, var = MSQ[l][0:KP], VAR[l][0:KP]
                scale, shift = SCALE[l][0:KP, u[1] % 2], SHIFT[l][0:KP, u[1] % 2]
                step(nc.gpsimd.tensor_tensor(t, s[:, :, 0:3], s[:, :, 3:6], ALU.add))
                step(nc.gpsimd.tensor_tensor(var, t[:, :, 0], t[:, :, 2], ALU.add))
                step(nc.gpsimd.tensor_tensor(msq, t[:, :, 1], t[:, :, 1], ALU.mult))
                step(nc.gpsimd.tensor_scalar(var, var, -2.0 / (CG * V), EPS, ALU.mult, ALU.add))
                step(nc.gpsimd.tensor_tensor(var, var, msq, ALU.subtract))
                step(nc.gpsimd.tensor_scalar(var, var, EPS, 1.0, ALU.max, ALU.mult))
                step(nc.gpsimd.tensor_tensor(scale, var, POWER[0:KP], ALU.pow))
                nc.gpsimd.tensor_tensor(shift, t[:, :, 1], scale, ALU.mult).then_inc(norm_ready[l], 1)

            def normalise(u, body):
                if known(u, body) >= 1:
                    wait_alone(conv0_done, count(u, CG))
                wait_alone(norm_ready[0], count(u, 1, 1))
                for b in range(NB):
                    nc.gpsimd.tensor_scalar(XN0[0:KP, :, b * V:(b + 1) * V], X[u[1]][0:KP, :, b, :],
                                                   SCALE[0][0:KP, u[1] % 2, b:b + 1],
                                                   SHIFT[0][0:KP, u[1] % 2, b:b + 1], ALU.mult, ALU.add)
                pe = PE[0:KP, bass.ds(CG * (u[0] * 2 + u[1] // 2), CG)]
                nc.gpsimd.tensor_copy(XN0[0:KP, :, N], pe).then_inc(xn_ready[0], 1)

            def slot(u, body=False):
                if exists(u, 2, body):
                    normalise(after(u, 2), body)
                if exists(u, 1, body):
                    scale_and_shift(1, after(u, 1), body)
                if exists(u, 3, body):
                    scale_and_shift(0, after(u, 3), body)

            scale_and_shift(0, (0, 0), False)
            normalise((0, 0), False)
            scale_and_shift(0, (0, 1), False)
            slots(pool, slot)


def kernel(x, L0_conv_pe, L0_conv_weight, L0_conv_bias, L1_conv_k):
    import numpy as np
    import concourse.bacc as bacc
    from concourse import mybir as my
    from concourse.bass_utils import run_bass_kernel_spmd

    x = np.asarray(x)
    pe, w, bias, k = (np.asarray(a) for a in (L0_conv_pe, L0_conv_weight, L0_conv_bias, L1_conv_k))
    B, C, H, W = x.shape

    x_rows = x.reshape(HALVES, NB, NGROUP, CG, H, V, 2).transpose(2, 0, 6, 4, 3, 1, 5)
    x_rows = np.ascontiguousarray(x_rows).reshape(UNITS, 2, H, CG * NB * V)
    i = np.arange(H)
    taps = w.reshape(C, H)
    t0 = taps[:, (i[:, None] - i[None, :]) % H].reshape(NGROUP, CG, H, H).transpose(0, 2, 1, 3)
    t0 = np.ascontiguousarray(t0)
    bias_rows = np.zeros((NGROUP, 1, CG, KP), bias.dtype)
    bias_rows[..., 0:H] = bias_rows[..., P_ODD:KP] = bias.reshape(NGROUP, 1, CG, 1)
    k3 = k.reshape(C, 3, 3)
    band = np.zeros((4, C, H, P_ODD), k.dtype)
    for s, dx in enumerate((1, 0, 2, 1)):
        for dy in range(3):
            h = i[(i - dy + 1 >= 0) & (i - dy + 1 < H)]
            band[s][:, h, h - dy + 1] = k3[:, dy, dx][:, None]
    t1 = np.ascontiguousarray(band.reshape(4, NGROUP, CG, H, P_ODD).transpose(1, 3, 2, 0, 4))
    pe_rows = np.ascontiguousarray(pe.reshape(C, H).T)

    nc = bacc.Bacc("TRN2", target_bir_lowering=False, num_devices=1)
    arrays, args = {}, []
    for name, a in (("x", x_rows), ("t0", t0), ("bias", bias_rows), ("t1", t1), ("pe", pe_rows)):
        arrays[name] = a
        args.append(nc.dram_tensor(name, a.shape, my.dt.from_np(a.dtype), kind="ExternalInput").ap())
    out = nc.dram_tensor("out", x_rows.shape, my.dt.from_np(x_rows.dtype), kind="ExternalOutput").ap()
    residual_convs(nc, *args, out)
    r = run_bass_kernel_spmd(nc, [arrays], core_ids=[0])
    y = r.results[0]["out"].reshape(NGROUP, HALVES, 2, H, CG, NB, V).transpose(1, 5, 0, 4, 3, 6, 2)
    return np.ascontiguousarray(y).reshape(B, C, H, W)
```

```python
from contextlib import ExitStack

import concourse.bass as bass
from concourse import mybir


P_ODD = 64
ROWS = 56
KP = P_ODD + ROWS
CG = 12
NB = 16
V = 28
N = NB * V
VP = V + 2
NCH = 384
NGROUP = NCH // CG
HALVES = 2
UNITS = NGROUP * HALVES
BANK = 512
EPS = 1e-5
PAIRS = CG // 2
NX = 4
PARTS = 3
CP = CG // PARTS
ACT_IMAGES = 6
SHARE = 8
W_DMAS = 5

F32 = mybir.dt.float32
ALU = mybir.AluOpType
ACT = mybir.ActivationFunctionType


def residual_convs(nc, x_h, t0_h, bias_h, t1_h, pe_h, out_h):
    with ExitStack() as ctx:
        def sb(name, shape):
            return ctx.enter_context(nc.sbuf_tensor(name, shape, F32))

        def ps(name, shape):
            return ctx.enter_context(nc.psum_tensor(name, shape, F32))

        def sem(name):
            return ctx.enter_context(nc.semaphore(name))

        X = [sb(f"X{k}", [128, CG, NB, V]) for k in range(NX)]
        XN0 = sb("XN0", [128, CG, N + 1])
        XN1 = [sb(f"XN1_{k}", [128, CG, NB, VP]) for k in range(2)]
        W0 = [sb(f"W0_{k}", [128, CG, KP]) for k in range(2)]
        W1 = [sb(f"W1_{k}", [128, CG, 4, P_ODD]) for k in range(2)]
        PE = sb("PE", [128, NCH])
        ST = [[sb(f"ST{l}_{k}", [128, NB, 6]) for k in range(2)] for l in range(2)]
        SUM = [sb(f"SUM{l}", [128, NB, 6]) for l in range(2)]
        TMP = [sb(f"TMP{l}", [128, NB, 3]) for l in range(2)]
        MSQ = [sb(f"MSQ{l}", [128, NB]) for l in range(2)]
        VAR = [sb(f"VAR{l}", [128, NB]) for l in range(2)]
        SCALE = [sb(f"SCALE{l}", [128, 2, NB]) for l in range(2)]
        SHIFT = [sb(f"SHIFT{l}", [128, 2, NB]) for l in range(2)]
        AVG = sb("AVG", [128, KP])
        SKIP = ctx.enter_context(nc.sbuf_tensor("SKIP", [128, ACT_IMAGES, 2, CG, V], mybir.dt.bfloat16))
        POWER = sb("POWER", [128, NB])

        conv0 = [ps(f"conv0_{k}", [128, BANK]) for k in range(3)]
        conv1 = [ps(f"conv1_{k}", [128, 2, BANK]) for k in range(2)]
        sums = ps("sums", [128, 2, NB * 6])

        x_loaded = [sem(f"x_loaded{k}") for k in range(NX)]
        x_stored = [[sem(f"x_stored{k}_{p}") for p in range(PARTS)] for k in range(NX)]
        w_loaded = [sem(f"w_loaded{k}") for k in range(2)]
        pe_loaded = sem("pe_loaded")
        x_cleared = [sem(f"x_cleared{k}") for k in range(NX)]
        w_cleared = [sem(f"w_cleared{k}") for k in range(2)]
        xn1_cleared = sem("xn1_cleared")
        st0_cleared = sem("st0_cleared")
        pe_filled = sem("pe_filled")
        avg_filled = sem("avg_filled")
        power_filled = sem("power_filled")
        stats_done = [sem(f"stats{l}_done") for l in range(2)]
        squares_done = [sem(f"squares{l}_done") for l in range(2)]
        sums_done = [sem(f"sums{l}_done") for l in range(2)]
        sums_copied = [sem(f"sums{l}_copied") for l in range(2)]
        norm_step = [sem(f"norm{l}_step") for l in range(2)]
        pool_passed = sem("pool_passed")
        norm_ready = [sem(f"norm{l}_ready") for l in range(2)]
        xn_ready = [sem(f"xn{l}_ready") for l in range(2)]
        xn_shared = [sem(f"xn{l}_shared") for l in range(2)]
        conv0_done = sem("conv0_done")
        x1_done = sem("x1_done")
        conv1_done = sem("conv1_done")
        x2_done = sem("x2_done")

        block = ctx.enter_context(nc.Block())

        def after(u, n):
            return (u[0] + (u[1] + n) // NX, (u[1] + n) % NX)

        def count(u, each=1, more=0):
            return u[0] * (NX * each) + (u[1] * each + more)

        def slots(eng, slot):
            slot((-1, 3))
            slot((0, 0))
            with eng.Fori(0, (UNITS - NX) // NX) as m:
                for r in range(1, NX + 1):
                    slot((m + r // NX, r % NX), body=True)
            for r in range(1, NX):
                slot((UNITS // NX - 1, r))

        def known(u, body):
            return UNITS // 2 if body else NX * u[0] + u[1]

        def exists(u, n, body):
            return 0 <= known(u, body) + n < UNITS

        @block.sync
        def _(sp):
            def load_x(u, parts=range(PARTS)):
                k = u[1]
                row = x_h[count(u)]
                for p in parts:
                    here = slice(p * CP, (p + 1) * CP)
                    for side, at in ((0, 0), (1, P_ODD)):
                        sp.dma_start(X[k][at:at + ROWS, here].rearrange("p c b v -> p (c b v)"),
                                     row[side, :, p * CP * N:(p + 1) * CP * N]).then_inc(x_loaded[k], 16)

            def store(u, p):
                k = u[1]
                row = out_h[count(u)]
                here = slice(p * CP, (p + 1) * CP)
                sp.wait_ge(x2_done, count(u, PAIRS, (p + 1) * CP // 2))
                for side, at in ((0, 0), (1, P_ODD)):
                    sp.dma_start(row[side, :, p * CP * N:(p + 1) * CP * N],
                                 X[k][at:at + ROWS, here].rearrange("p c b v -> p (c b v)"),
                                 ).then_inc(x_stored[k][p], 16)

            def reload(u, p):
                sp.wait_ge(x_stored[u[1]][p], 32 * u[0] + 32)
                load_x(after(u, NX), (p,))

            def load_w(g, j):
                done = w_loaded[j]
                sp.dma_start(W0[j][0:ROWS, :, 0:ROWS], t0_h[g]).then_inc(done, 16)
                sp.dma_start(W0[j][P_ODD:KP, :, P_ODD:KP], t0_h[g]).then_inc(done, 16)
                sp.dma_start(W0[j][ROWS:ROWS + 1, :, :], bias_h[g]).then_inc(done, 16)
                sp.dma_start(W1[j][0:ROWS, :, 1:4, :].rearrange("p c s i -> p c (s i)"),
                             t1_h[g][:, :, 0:3, :].rearrange("p c s i -> p c (s i)")).then_inc(done, 16)
                sp.dma_start(W1[j][P_ODD:KP, :, 0:3, :].rearrange("p c s i -> p c (s i)"),
                             t1_h[g][:, :, 1:4, :].rearrange("p c s i -> p c (s i)")).then_inc(done, 16)

            def store_and_reload(u):
                for p in range(PARTS):
                    store(u, p)
                    if p > 0:
                        reload(u, p - 1)
                reload(u, PARTS - 1)
                if u[1] % 2:
                    load_w(u[0] * 2 + (u[1] // 2 + 2), u[1] // 2)

            sp.wait_ge(x_cleared[0], 2)
            load_x((0, 0))
            sp.wait_ge(pe_filled, 1)
            sp.dma_start(PE[0:ROWS, :], pe_h).then_inc(pe_loaded, 16)
            sp.dma_start(PE[P_ODD:KP, :], pe_h).then_inc(pe_loaded, 16)
            sp.wait_ge(w_cleared[0], 2)
            load_w(0, 0)
            for k in range(1, NX):
                sp.wait_ge(x_cleared[k], 1)
                load_x((0, k))
                if k == 1:
                    sp.wait_ge(w_cleared[1], 2)
                    load_w(1, 1)
            with sp.Fori(0, UNITS // NX - 1) as m:
                for r in range(NX):
                    store_and_reload((m, r))
            for r in range(NX):
                for p in range(PARTS):
                    store((UNITS // NX - 1, r), p)
            for k in range(NX):
                for p in range(PARTS):
                    sp.wait_ge(x_stored[k][p], 32 * (UNITS // NX))

        @block.vector
        def _(dve):
            nc.vector.memset(X[0][:, 0:PAIRS], 0.0).then_inc(x_cleared[0], 1)
            for k in range(2):
                nc.vector.memset(W0[k][:], 0.0).then_inc(w_cleared[k], 1)
                nc.vector.memset(W1[k][:], 0.0).then_inc(w_cleared[k], 1)

            def statistics(l, u, body, images):
                for b in images:
                    if b == (0 if l else ACT_IMAGES):
                        if l == 0:
                            dve.wait_ge(x_loaded[u[1]], 32 * PARTS * u[0] + 32 * PARTS)
                        else:
                            dve.wait_ge(x1_done, count(u, CG, CG))
                        if known(u, body) >= 2:
                            dve.wait_ge(sums_done[l], count(u, 1, -1))
                    last = nc.vector.bn_stats(ST[l][u[1] % 2][0:KP, b, :], X[u[1]][0:KP, :, b, :])
                    if b == NB - 1:
                        last.then_inc(stats_done[l], 1)

            def add_conv0(u, c):
                bank = conv0[c % 3]
                dve.wait_ge(conv0_done, count(u, CG, c + 1))
                x = X[u[1]][0:KP, c].rearrange("p b v -> p (b v)")
                nc.vector.scalar_tensor_tensor(out=x, in0=bank[0:KP, 0:N], scalar=bank[0:KP, N:N + 1], in1=x,
                                               op0=ALU.add, op1=ALU.add).then_inc(x1_done, 1)

            def add_conv1(u, j):
                dve.wait_ge(conv1_done, count(u, PAIRS, j + 1))
                x = X[u[1]][0:KP, 2 * j:2 * j + 2].rearrange("p c b v -> p c (b v)")
                nc.vector.tensor_tensor(x, conv1[j % 2][0:KP, :, 0:N], x, ALU.add).then_inc(x2_done, 1)

            def slot(u, body=False):
                if exists(u, 1, body):
                    for c in range(CG):
                        add_conv0(after(u, 1), c)
                if known(u, body) == 0:
                    statistics(0, after(u, 2), body, range(ACT_IMAGES, NB))
                for j in range(PAIRS):
                    if j < 3 and exists(u, 1, body):
                        statistics(1, after(u, 1), body, range(NB * j // 3, NB * (j + 1) // 3))
                    if j >= 3 and exists(u, 3, body) and known(u, body) >= 0:
                        n = NB - ACT_IMAGES
                        statistics(0, after(u, 3), body,
                                   range(ACT_IMAGES + n * (j - 3) // 3, ACT_IMAGES + n * (j - 2) // 3))
                    if exists(u, 0, body):
                        add_conv1(u, j)

            dve.wait_ge(st0_cleared, 2)
            for k in range(2):
                statistics(0, (0, k), False, range(ACT_IMAGES, NB))
                if k == 0:
                    nc.vector.memset(X[2][:], 0.0).then_inc(x_cleared[2], 1)
            slots(dve, slot)

        def sum_statistics(pe, l, u, body):
            pe.wait_ge(squares_done[l], count(u, 1, 1))
            if l == 0 and known(u, body) == 1:
                pe.wait_ge(sums_copied[0], 1)
            elif l == 0 and known(u, body) >= 2:
                pe.wait_ge(sums_copied[1], count(u, 1, -1))
            elif l == 1 and exists(u, 1, body):
                pe.wait_ge(sums_copied[0], count(u, 1, 2))
            elif l == 1:
                pe.wait_ge(sums_copied[1], count(u))
            nc.tensor.matmul(sums[0:KP, l, :], AVG[0:KP, :],
                             ST[l][u[1] % 2][0:KP].rearrange("p b s -> p (b s)"),
                             start=True, stop=True).then_inc(sums_done[l], 1)

        @block.tensor
        def _(pe):
            def layer0(u, body, c):
                g = (u[1] // 2) % 2
                if c == 0:
                    pe.wait_ge(xn_ready[0], count(u, 1, 1))
                    if known(u, body) < 2:
                        pe.wait_ge(xn_shared[0], count(u, 1, 1))
                    pe.wait_ge(w_loaded[g], 16 * W_DMAS * u[0] + 16 * W_DMAS)
                if known(u, body) * CG + c >= 3:
                    pe.wait_ge(x1_done, count(u, CG, c - 2))
                nc.tensor.matmul(conv0[c % 3][0:KP, 0:N + 1], W0[g][0:KP, c, :], XN0[0:KP, c, :],
                                 start=True, stop=True).then_inc(conv0_done, 1)

            def layer1(u, body, j):
                g = (u[1] // 2) % 2
                if j == 0:
                    pe.wait_ge(xn_ready[1], count(u, 1, 1))
                    if known(u, body) == 0:
                        pe.wait_ge(xn_shared[1], 1)
                if known(u, body) * PAIRS + j >= 2:
                    pe.wait_ge(x2_done, count(u, PAIRS, j - 1))
                for i in range(2):
                    if i == 1 and j == 3 and exists(u, 1, body):
                        sum_statistics(pe, 1, after(u, 1), body)
                    c = 2 * j + i
                    even = conv1[j % 2][0:P_ODD, i, 0:N]
                    odd = conv1[j % 2][P_ODD:KP, i, 0:N]
                    for part in range(2):
                        for out, side in ((even, 0), (odd, 1)):
                            last = nc.tensor.matmul(out, W1[g][0:KP, c, 2 * side + part, 0:out.shape[0]],
                                                    XN1[u[1] % 2][0:KP, c, :, side + part:side + part + V],
                                                    start=part == 0, stop=part == 1)
                last.then_inc(conv1_done, 1)

            def slot(u, body=False):
                filling = known(u, body) == 0
                if exists(u, 1, body):
                    for c in range(CG):
                        layer0(after(u, 1), body, c)
                        if c == 3 and filling:
                            sum_statistics(pe, 1, u, body)
                        if c == (CG - 1 if filling else 5) and exists(u, 2, body):
                            sum_statistics(pe, 0, after(u, 2), body)
                if exists(u, 0, body):
                    for j in range(PAIRS):
                        layer1(u, body, j)

            pe.wait_ge(avg_filled, 3)
            sum_statistics(pe, 0, (0, 0), False)
            pe.wait_ge(xn1_cleared, 2)
            pe.wait_ge(pe_loaded, 32)
            slots(pe, slot)

        @block.scalar
        def _(act):
            def squares(l, u):
                first = ACT_IMAGES if l == 0 else 0
                st = ST[l][u[1] % 2][0:KP, first:].rearrange("p b (a s) -> p b a s", a=2)
                act.wait_ge(stats_done[l], count(u, 1, 1))
                nc.scalar.activation(st[:, :, :, 0], st[:, :, :, 1], ACT.Square,
                                     scale=float(CG * V / 2) ** 0.5).then_inc(squares_done[l], 1)

            def statistics0(u, body, images):
                for b in images:
                    if b == 0:
                        act.wait_ge(x_loaded[u[1]], 32 * PARTS * u[0] + 32 * PARTS)
                        if known(u, body) >= 2:
                            act.wait_ge(sums_done[0], count(u, 1, -1))
                        if known(u, body) >= 1:
                            act.wait_ge(squares_done[0], count(u))
                    x = X[u[1]][0:KP, :, b, :]
                    st = ST[0][u[1] % 2]
                    nc.scalar.activation(SKIP[0:KP, b, 0], x, ACT.Square, accum_out=st[0:KP, b, 0:1])
                    nc.scalar.activation(SKIP[0:KP, b, 1], x, ACT.Copy, scale=2.0 / (CG * V),
                                         accum_out=st[0:KP, b, 1:2])

            def copy_sums(l, u, body):
                act.wait_ge(sums_done[l], count(u, 1, 1))
                if known(u, body) >= 1:
                    act.wait_ge(norm_ready[l], count(u))
                nc.scalar.activation(SUM[l][0:KP].rearrange("p b s -> p (b s)"), sums[0:KP, l, :],
                                     ACT.Copy).then_inc(sums_copied[l], 1)

            def normalise(u, body, images):
                for b in images:
                    if b == 0:
                        act.wait_ge(norm_ready[1], count(u, 1, 1))
                        if known(u, body) >= 2:
                            act.wait_ge(conv1_done, count(u, PAIRS, -PAIRS))
                    last = nc.scalar.activation(XN1[u[1] % 2][0:KP, :, b, 1:1 + V], X[u[1]][0:KP, :, b, :],
                                                ACT.Identity, bias=SHIFT[1][0:KP, u[1] % 2, b:b + 1],
                                                scale=SCALE[1][0:KP, u[1] % 2, b:b + 1])
                    if b == (SHARE if known(u, body) == 0 else NB) - 1:
                        last.then_inc(xn_ready[1], 1)

            def share(u):
                act.wait_ge(norm_ready[0], count(u, 1, 1))
                if u[1] > 0:
                    act.wait_ge(conv0_done, count(u, CG))
                for b in range(SHARE, NB):
                    last = nc.scalar.activation(XN0[0:KP, :, b * V:(b + 1) * V], X[u[1]][0:KP, :, b, :],
                                                ACT.Identity, bias=SHIFT[0][0:KP, u[1], b:b + 1],
                                                scale=SCALE[0][0:KP, u[1], b:b + 1])
                last.then_inc(xn_shared[0], 1)

            def slot(u, body=False):
                if exists(u, 3, body):
                    statistics0(after(u, 3), body, range(ACT_IMAGES))
                filling = known(u, body) == -1
                if filling:
                    share(after(u, 2))
                if exists(u, 1, body):
                    squares(1, after(u, 1))
                    copy_sums(1, after(u, 1), body)
                    normalise(after(u, 1), body, range(8))
                if exists(u, 3, body):
                    squares(0, after(u, 3))
                if exists(u, 1, body) and not filling:
                    normalise(after(u, 1), body, range(8, 14))
                if exists(u, 3, body):
                    copy_sums(0, after(u, 3), body)
                if exists(u, 1, body) and not filling:
                    normalise(after(u, 1), body, range(14, NB))

            act.wait_ge(st0_cleared, 2)
            for k in range(2):
                statistics0((0, k), False, range(ACT_IMAGES))
                if k == 1:
                    act.wait_ge(xn1_cleared, 2)
                squares(0, (0, k))
                copy_sums(0, (0, k), False)
                if k == 0:
                    share((0, 0))
            slots(act, slot)

        @block.gpsimd
        def _(pool):
            nc.gpsimd.memset(X[0][:, PAIRS:CG], 0.0).then_inc(x_cleared[0], 1)
            nc.gpsimd.memset(AVG[:, 0:ROWS], -1.0 / (2 * 2 * ROWS)).then_inc(avg_filled, 1)
            nc.gpsimd.memset(AVG[:, ROWS:P_ODD], 0.0).then_inc(avg_filled, 1)
            nc.gpsimd.memset(AVG[:, P_ODD:KP], -1.0 / (2 * 2 * ROWS)).then_inc(avg_filled, 1)
            nc.gpsimd.memset(PE[:], 1.0).then_inc(pe_filled, 1)
            nc.gpsimd.memset(POWER[:], -0.5).then_inc(power_filled, 1)
            for k in range(2):
                nc.gpsimd.memset(ST[0][k][:], 0.0).then_inc(st0_cleared, 1)
            nc.gpsimd.memset(X[1][:], 0.0).then_inc(x_cleared[1], 1)
            for k in range(2):
                nc.gpsimd.memset(XN1[k][:, :, :, 0:VP:VP - 1], 0.0).then_inc(xn1_cleared, 1)
            nc.gpsimd.memset(X[3][:], 0.0).then_inc(x_cleared[3], 1)
            pool.wait_ge(power_filled, 1)
            pool.wait_ge(pe_loaded, 32)
            STEPS = 7

            def wait_alone(sem, value):
                pool.wait_ge(sem, value)
                pool.sem_inc(pool_passed, 1)

            def scale_and_shift(l, u, body):
                steps = [0]

                def step(instruction):
                    instruction.then_inc(norm_step[l], 1)
                    steps[0] += 1
                    wait_alone(norm_step[l], count(u, STEPS, steps[0]))

                pool.wait_ge(sums_copied[l], count(u, 1, 1))
                if l == 1 and known(u, body) >= 2:
                    pool.wait_ge(xn_ready[1], count(u, 1, -1))
                s, t = SUM[l][0:KP], TMP[l][0:KP]
                msq, var = MSQ[l][0:KP], VAR[l][0:KP]
                scale, shift = SCALE[l][0:KP, u[1] % 2], SHIFT[l][0:KP, u[1] % 2]
                step(nc.gpsimd.tensor_tensor(t, s[:, :, 0:3], s[:, :, 3:6], ALU.add))
                step(nc.gpsimd.tensor_tensor(var, t[:, :, 0], t[:, :, 2], ALU.add))
                step(nc.gpsimd.tensor_tensor(msq, t[:, :, 1], t[:, :, 1], ALU.mult))
                step(nc.gpsimd.tensor_scalar(var, var, -2.0 / (CG * V), EPS, ALU.mult, ALU.add))
                step(nc.gpsimd.tensor_tensor(var, var, msq, ALU.subtract))
                step(nc.gpsimd.tensor_scalar(var, var, EPS, 1.0, ALU.max, ALU.mult))
                step(nc.gpsimd.tensor_tensor(scale, var, POWER[0:KP], ALU.pow))
                nc.gpsimd.tensor_tensor(shift, t[:, :, 1], scale, ALU.mult).then_inc(norm_ready[l], 1)

            def normalise(u, body):
                if known(u, body) >= 1:
                    wait_alone(conv0_done, count(u, CG))
                wait_alone(norm_ready[0], count(u, 1, 1))
                for b in range(SHARE if known(u, body) < 2 else NB):
                    nc.gpsimd.tensor_scalar(XN0[0:KP, :, b * V:(b + 1) * V], X[u[1]][0:KP, :, b, :],
                                                   SCALE[0][0:KP, u[1] % 2, b:b + 1],
                                                   SHIFT[0][0:KP, u[1] % 2, b:b + 1], ALU.mult, ALU.add)
                pe = PE[0:KP, bass.ds(CG * (u[0] * 2 + u[1] // 2), CG)]
                nc.gpsimd.tensor_copy(XN0[0:KP, :, N], pe).then_inc(xn_ready[0], 1)

            def share():
                pool.wait_ge(xn1_cleared, 2)
                pool.wait_ge(norm_ready[1], 1)
                for b in range(SHARE, NB):
                    last = nc.gpsimd.tensor_scalar(XN1[0][0:KP, :, b, 1:1 + V], X[0][0:KP, :, b, :],
                                                   SCALE[1][0:KP, 0, b:b + 1], SHIFT[1][0:KP, 0, b:b + 1],
                                                   ALU.mult, ALU.add)
                last.then_inc(xn_shared[1], 1)

            def slot(u, body=False):
                if exists(u, 2, body):
                    normalise(after(u, 2), body)
                if exists(u, 1, body):
                    scale_and_shift(1, after(u, 1), body)
                if known(u, body) == -1:
                    share()
                if exists(u, 3, body):
                    scale_and_shift(0, after(u, 3), body)

            scale_and_shift(0, (0, 0), False)
            normalise((0, 0), False)
            scale_and_shift(0, (0, 1), False)
            slots(pool, slot)


def kernel(x, L0_conv_pe, L0_conv_weight, L0_conv_bias, L1_conv_k):
    import numpy as np
    import concourse.bacc as bacc
    from concourse import mybir as my
    from concourse.bass_utils import run_bass_kernel_spmd

    x = np.asarray(x)
    pe, w, bias, k = (np.asarray(a) for a in (L0_conv_pe, L0_conv_weight, L0_conv_bias, L1_conv_k))
    B, C, H, W = x.shape

    x_rows = x.reshape(HALVES, NB, NGROUP, CG, H, V, 2).transpose(2, 0, 6, 4, 3, 1, 5)
    x_rows = np.ascontiguousarray(x_rows).reshape(UNITS, 2, H, CG * NB * V)
    i = np.arange(H)
    taps = w.reshape(C, H)
    t0 = taps[:, (i[:, None] - i[None, :]) % H].reshape(NGROUP, CG, H, H).transpose(0, 2, 1, 3)
    t0 = np.ascontiguousarray(t0)
    bias_rows = np.zeros((NGROUP, 1, CG, KP), bias.dtype)
    bias_rows[..., 0:H] = bias_rows[..., P_ODD:KP] = bias.reshape(NGROUP, 1, CG, 1)
    k3 = k.reshape(C, 3, 3)
    band = np.zeros((4, C, H, P_ODD), k.dtype)
    for s, dx in enumerate((1, 0, 2, 1)):
        for dy in range(3):
            h = i[(i - dy + 1 >= 0) & (i - dy + 1 < H)]
            band[s][:, h, h - dy + 1] = k3[:, dy, dx][:, None]
    t1 = np.ascontiguousarray(band.reshape(4, NGROUP, CG, H, P_ODD).transpose(1, 3, 2, 0, 4))
    pe_rows = np.ascontiguousarray(pe.reshape(C, H).T)

    nc = bacc.Bacc("TRN2", target_bir_lowering=False, num_devices=1)
    arrays, args = {}, []
    for name, a in (("x", x_rows), ("t0", t0), ("bias", bias_rows), ("t1", t1), ("pe", pe_rows)):
        arrays[name] = a
        args.append(nc.dram_tensor(name, a.shape, my.dt.from_np(a.dtype), kind="ExternalInput").ap())
    out = nc.dram_tensor("out", x_rows.shape, my.dt.from_np(x_rows.dtype), kind="ExternalOutput").ap()
    residual_convs(nc, *args, out)
    r = run_bass_kernel_spmd(nc, [arrays], core_ids=[0])
    y = r.results[0]["out"].reshape(NGROUP, HALVES, 2, H, CG, NB, V).transpose(1, 5, 0, 4, 3, 6, 2)
    return np.ascontiguousarray(y).reshape(B, C, H, W)
```
